# Optimizing a Trainium2 kernel written in Bass

```python
import numpy as np
import jax
import jax.numpy as jnp

def _softmax(x, axis=-1):
    return jax.nn.softmax(x, axis=axis)

def _gelu(x):
    return jax.nn.gelu(x, approximate=True)

def _silu(x):
    return jax.nn.silu(x)

def _sigmoid(x):
    return jax.nn.sigmoid(x)

def _layernorm(x, axis=-1, eps=1e-05):
    m = jnp.mean(x, axis=axis, keepdims=True)
    v = jnp.var(x, axis=axis, keepdims=True)
    return (x - m) / jnp.sqrt(v + eps)

def _scatter_add(tgt, idx, src, axis=0):
    return tgt.at[idx].add(src)

def _segment_sum(src, seg, n):
    return jax.ops.segment_sum(src, seg, n)
kernel_name = 'mk_gps_d1_gnn_r8_b6963d'

def setup_inputs(seed: int=0):
    np.random.seed(seed)
    _w = jnp.asarray

    def _rec_inputs():
        import jax
        import jax.numpy as jnp
        _gk = jax.random.key(seed)
        x = -8.776e-05 + 1 * jax.random.normal(jax.random.fold_in(_gk, 1), (1250, 512), jnp.float32)
        src = jax.random.randint(jax.random.fold_in(_gk, 2), (20000,), 0, 1250, jnp.int32)
        dst = jnp.minimum((1250 * jax.random.uniform(jax.random.fold_in(_gk, 3), (20000,)) ** 2.0).astype(jnp.int32), 9999)
        _o = jnp.argsort(dst, stable=True)
        src = src[_o]
        dst = dst[_o]
        return (x, src, dst)
    x, src, dst = _rec_inputs()

    def _L0_gnn_setup():
        import jax, jax.numpy as jnp
        import numpy as np
        N_NODES = 1250

        def gcn_layer(x, src, dst, W, b, num_nodes):
            h = x @ W
            loop = jnp.arange(num_nodes, dtype=src.dtype)
            src_f = jnp.concatenate([src, loop])
            dst_f = jnp.concatenate([dst, loop])
            ones = jnp.ones(src_f.shape[0], dtype=h.dtype)
            deg = jax.ops.segment_sum(ones, dst_f, num_segments=num_nodes)
            dinv = jnp.where(deg > 0, jax.lax.rsqrt(deg), 0.0)
            norm = dinv[src_f] * dinv[dst_f]
            msg = h[src_f] * norm[:, None]
            out = jax.ops.segment_sum(msg, dst_f, num_segments=num_nodes)
            return out + b
        key = jax.random.key(seed)
        k = jax.random.split(key, 6)
        N, E, D, H, O = (N_NODES, 20000, 512, 1024, 512)
        x = jax.random.normal(k[0], (N, D), dtype=jnp.float32)
        edge_index = jax.random.randint(k[1], (2, E), 0, N, dtype=jnp.int64)
        W1 = jax.random.normal(k[2], (D, H), dtype=jnp.float32) * (1.0 / np.sqrt(D))
        b1 = jnp.zeros((H,), dtype=jnp.float32)
        W2 = jax.random.normal(k[3], (H, O), dtype=jnp.float32) * (1.0 / np.sqrt(H))
        b2 = jnp.zeros((O,), dtype=jnp.float32)
        return {'x': x, 'edge_index': edge_index, 'W1': W1, 'b1': b1, 'W2': W2, 'b2': b2}
    _L0_gnn_all = _L0_gnn_setup()
    _L0_gnn_in = {k: v for k, v in _L0_gnn_all.items() if k in ('W1', 'b1', 'W2', 'b2')}
    del _L0_gnn_all

    def _L0_mix_setup():
        import jax, jax.numpy as jnp
        import numpy as np
        HEADS = 8
        DIM_HEAD = 64
        DIM = 512
        INNER = HEADS * DIM_HEAD
        SCALE = DIM_HEAD ** (-0.5)

        def _feature_map(t):
            return jax.nn.elu(t) + 1.0
        key = jax.random.key(seed)
        k1, k2, k3, k4 = jax.random.split(key, 4)
        b, n = (8, 512)
        x = jax.random.normal(k1, (b, n, DIM), dtype=jnp.float32)
        w_qkv = jax.random.normal(k2, (INNER * 3, DIM), dtype=jnp.float32) * DIM ** (-0.5)
        w_out = jax.random.normal(k3, (DIM, INNER), dtype=jnp.float32) * INNER ** (-0.5)
        b_out = jax.random.normal(k4, (DIM,), dtype=jnp.float32) * 0.01
        return {'x': x, 'w_qkv': w_qkv, 'w_out': w_out, 'b_out': b_out}
    _L0_mix_all = _L0_mix_setup()
    _L0_mix_in = {k: v for k, v in _L0_mix_all.items() if k in ('w_qkv', 'w_out', 'b_out')}
    del _L0_mix_all

    def _L0_ffn_setup():
        import jax, jax.numpy as jnp
        import numpy as np
        EPS = 1e-09
        LN_EPS = 1e-05

        def _layernorm(x, gamma):
            x = x.astype(jnp.float32)
            mu = jnp.mean(x, axis=-1, keepdims=True)
            var = jnp.var(x, axis=-1, keepdims=True)
            return (x - mu) * jax.lax.rsqrt(var + LN_EPS) * gamma
        key = jax.random.key(seed)
        ks = jax.random.split(key, 5)
        b, n, d, e, h = (4, 1024, 512, 6, 256)
        x = jax.random.normal(ks[0], (b, n, d), dtype=jnp.float32)
        w_gating = jax.random.normal(ks[1], (d, e), dtype=jnp.float32)
        std1 = 1.0 / np.sqrt(h)
        std2 = 1.0 / np.sqrt(d)
        w1 = jax.random.uniform(ks[2], (e, d, h), jnp.float32, -std1, std1)
        w2 = jax.random.uniform(ks[3], (e, h, d), jnp.float32, -std2, std2)
        gamma = jnp.ones((d,), dtype=jnp.float32)
        return {'x': x, 'w_gating': w_gating, 'gamma': gamma, 'w1': w1, 'w2': w2}
    _L0_ffn_all = _L0_ffn_setup()
    _L0_ffn_in = {k: v for k, v in _L0_ffn_all.items() if k in ('w_gating', 'gamma', 'w1', 'w2')}
    del _L0_ffn_all
    return {'x': x, 'src': src, 'dst': dst, 'L0_gnn_W1': _L0_gnn_in['W1'], 'L0_gnn_b1': _L0_gnn_in['b1'], 'L0_gnn_W2': _L0_gnn_in['W2'], 'L0_gnn_b2': _L0_gnn_in['b2'], 'L0_mix_w_qkv': _L0_mix_in['w_qkv'], 'L0_mix_w_out': _L0_mix_in['w_out'], 'L0_mix_b_out': _L0_mix_in['b_out'], 'L0_ffn_w_gating': _L0_ffn_in['w_gating'], 'L0_ffn_gamma': _L0_ffn_in['gamma'], 'L0_ffn_w1': _L0_ffn_in['w1'], 'L0_ffn_w2': _L0_ffn_in['w2']}

def reference(x, src, dst, L0_gnn_W1, L0_gnn_b1, L0_gnn_W2, L0_gnn_b2, L0_mix_w_qkv, L0_mix_w_out, L0_mix_b_out, L0_ffn_w_gating, L0_ffn_gamma, L0_ffn_w1, L0_ffn_w2):
    import jax
    import jax.numpy as jnp

    def _L0_gnn_ref(x, edge_index, W1, b1, W2, b2):
        import jax, jax.numpy as jnp
        import numpy as np
        N_NODES = 1250

        def gcn_layer(x, src, dst, W, b, num_nodes):
            h = x @ W
            loop = jnp.arange(num_nodes, dtype=src.dtype)
            src_f = jnp.concatenate([src, loop])
            dst_f = jnp.concatenate([dst, loop])
            ones = jnp.ones(src_f.shape[0], dtype=h.dtype)
            deg = jax.ops.segment_sum(ones, dst_f, num_segments=num_nodes)
            dinv = jnp.where(deg > 0, jax.lax.rsqrt(deg), 0.0)
            norm = dinv[src_f] * dinv[dst_f]
            msg = h[src_f] * norm[:, None]
            out = jax.ops.segment_sum(msg, dst_f, num_segments=num_nodes)
            return out + b
        src, dst = (edge_index[0], edge_index[1])
        h = gcn_layer(x, src, dst, W1, b1, N_NODES)
        h = jax.nn.relu(h)
        out = gcn_layer(h, src, dst, W2, b2, N_NODES)
        return out

    def _L0_mix_ref(x, w_qkv, w_out, b_out):
        import jax, jax.numpy as jnp
        import numpy as np
        HEADS = 8
        DIM_HEAD = 64
        DIM = 512
        INNER = HEADS * DIM_HEAD
        SCALE = DIM_HEAD ** (-0.5)

        def _feature_map(t):
            return jax.nn.elu(t) + 1.0
        b, n, _ = x.shape
        h, d = (HEADS, DIM_HEAD)
        qkv = x @ w_qkv.T
        q, k, v = jnp.split(qkv, 3, axis=-1)
        reshape = lambda t: t.reshape(b, n, h, d).transpose(0, 2, 1, 3)
        q, k, v = (reshape(q), reshape(k), reshape(v))
        q = _feature_map(q * SCALE)
        k = _feature_map(k)
        k_cumsum = k.sum(axis=2)
        context = jnp.einsum('bhnd,bhne->bhde', k, v)
        out = jnp.einsum('bhnd,bhde->bhne', q, context)
        denom = jnp.einsum('bhnd,bhd->bhn', q, k_cumsum)[..., None] + 1e-08
        out = out / denom
        out = out.transpose(0, 2, 1, 3).reshape(b, n, h * d)
        return out @ w_out.T + b_out

    def _L0_ffn_ref(x, w_gating, gamma, w1, w2):
        import jax, jax.numpy as jnp
        import numpy as np
        EPS = 1e-09
        LN_EPS = 1e-05

        def _layernorm(x, gamma):
            x = x.astype(jnp.float32)
            mu = jnp.mean(x, axis=-1, keepdims=True)
            var = jnp.var(x, axis=-1, keepdims=True)
            return (x - mu) * jax.lax.rsqrt(var + LN_EPS) * gamma
        b, n, d = x.shape
        E = w_gating.shape[-1]
        C = max(min(n, int(n * 6.0 / E)), 4)
        raw = jnp.einsum('bnd,de->bne', x, w_gating)
        probs = jax.nn.softmax(raw, axis=-1)
        gate1 = jnp.max(probs, axis=-1)
        idx1 = jnp.argmax(probs, axis=-1)
        mask1 = jax.nn.one_hot(idx1, E, dtype=jnp.float32)
        gates_wo1 = probs * (1.0 - mask1)
        gate2 = jnp.max(gates_wo1, axis=-1)
        denom = gate1 + gate2 + EPS
        gate1 = gate1 / denom
        pos1 = (jnp.cumsum(mask1, axis=-2) - mask1) * mask1
        mask1 = mask1 * (pos1 < float(C)).astype(jnp.float32)
        mask1_flat = jnp.sum(mask1, axis=-1)
        pos1_flat = jnp.sum(pos1, axis=-1).astype(jnp.int32)
        gate1 = gate1 * mask1_flat
        combine = gate1[..., None, None] * mask1_flat[..., None, None] * jax.nn.one_hot(idx1, E, dtype=jnp.float32)[..., None] * jax.nn.one_hot(pos1_flat, C, dtype=jnp.float32)[..., None, :]
        dispatch = (combine != 0).astype(jnp.float32)
        expert_in = jnp.einsum('bnd,bnec->ebcd', x, dispatch)
        xn = _layernorm(expert_in, gamma)
        hidden = jax.nn.gelu(jnp.einsum('ebcd,edh->ebch', xn, w1), approximate=False)
        expert_out = jnp.einsum('ebch,ehd->ebcd', hidden, w2)
        out = jnp.einsum('ebcd,bnec->bnd', expert_out, combine)
        return out
    edge_index = jnp.stack([src, dst])
    xn = _layernorm(x, axis=-1)
    x = x + _L0_gnn_ref(xn, edge_index, L0_gnn_W1, L0_gnn_b1, L0_gnn_W2, L0_gnn_b2) + _L0_mix_ref(xn[None], L0_mix_w_qkv, L0_mix_w_out, L0_mix_b_out)[0]
    x = x + _L0_ffn_ref(_layernorm(x, axis=-1)[None], L0_ffn_w_gating, L0_ffn_gamma, L0_ffn_w1, L0_ffn_w2)[0]
    return x

_drawn_inputs = setup_inputs


def setup_inputs(seed=0):
    import zlib

    import numpy as np

    out = dict(_drawn_inputs(seed))
    spreads = {'L0_gnn_b1': (0.0, 0.1), 'L0_gnn_b2': (0.0, 0.1), 'L0_ffn_gamma': (1.0, 0.2)}
    factors = {'L0_mix_b_out': 4.306}
    for name, (base, spread) in spreads.items():
        noise = np.random.default_rng([zlib.crc32(name.encode()), seed]).standard_normal(out[name].shape)
        drawn = base * np.exp(spread * noise) if base else spread * noise
        out[name] = jnp.asarray(drawn.astype(out[name].dtype))
    for name, factor in factors.items():
        out[name] = (out[name] * factor).astype(out[name].dtype)
    return out
```

```python
import concourse.bass as bass
from concourse import mybir
from contextlib import ExitStack, contextmanager


class Steps:

    def __init__(self, eng, sem):
        self.eng, self.sem, self.n, self.i, self.per = eng, sem, 0, None, 0

    def mark(self, ins):
        ins.then_inc(self.sem, 1)
        self.n += 1

    def wait(self):
        self.eng.wait_ge(self.sem, self.n if self.i is None else self.i * self.per + self.n)

    def link(self, ins):
        self.mark(ins)
        self.wait()

    @contextmanager
    def loop(self, count, per):
        base = self.n
        with self.eng.Fori(0, count) as i:
            self.i, self.per = i, per
            yield i
            self.i = None
            assert self.n - base == per, (self.n - base, per)
        self.n = base + count * per


def gps_layer_kernel(nc, x_d, src_d, dst_d, dstt_d, W1_d, b1_d, W2_d, b2_d, wqkv_d, wout_d, bout_d, wg_d, gamma_d,
                     w1_d, w2_d, out_d, slots_d, yslots_d):
    fp32, fp16, i32, i16 = mybir.dt.float32, mybir.dt.float16, mybir.dt.int32, mybir.dt.int16
    ALU, ACT, AX = mybir.AluOpType, mybir.ActivationFunctionType, mybir.AxisListType
    ds = bass.ds

    N, D = x_d.shape
    H = W1_d.shape[1]
    EX, HE = w1_d.shape[0], w1_d.shape[2]
    B = 125
    NB = N // B
    KC, HC, EC = D // 128, H // 128, HE // 128
    ET = src_d.shape[1]
    TT = 2
    R = 8 // TT
    WIN = [(0, 4), (4, 4), (8, 2)]
    CH = [(0, 417), (417, 417), (834, 416)]
    P2 = NB // 2
    S6 = 64.0
    UN = 1.0 / (S6 * S6)
    EPS = 1e-5
    DH = 64
    QS = DH ** -0.5
    TS = 128
    NT = 16
    BIG = 12582912.0
    EXACT = 2048.0
    KTILE = S6 * N
    BDS = 1.0 / (KTILE * 1024.0)
    CXS = 1.0 / (16.0 * N)

    base = 16512
    PP = base
    Q = PP + 50048
    RR = Q + 57344
    S = RR + 20480
    T = S + 20480
    WO = T + 20480
    X = WO + 8192
    MI = X + 20480
    at = [MI]

    def sb(name, shape, dt, off):
        return nc.alloc_sbuf_tensor_at(name, shape, dt, offset=off)

    def misc(name, shape, dt):
        n = mybir.dt.size(dt) if hasattr(mybir.dt, "size") else {fp32: 4, i32: 4, fp16: 2, i16: 2}[dt]
        for s in shape[1:]:
            n *= s
        off = at[0]
        at[0] += (n + 31) // 32 * 32
        assert at[0] <= 229368, name
        return sb(name, shape, dt, off)

    xnT = sb("xnT", [128, KC, 2, N], fp16, PP)
    wqkv = sb("wqkv", [128, KC, 2, 3 * D], fp16, PP + 20032)
    Chi = sb("Chi", [B, NB, N], fp16, PP)
    Clo = sb("Clo", [B, NB, N], fp16, PP + 25024)
    oneb = sb("oneb", [B, ET * B], fp16, Q)
    ring = sb("ring", [B, R * TT * N], fp16, RR)
    colw = sb("colw", [B, NB, B], i16, Q + 44096)
    strip = sb("strip", [B, 2 * N - B], fp16, Q + 46656)
    sel = sb("sel", [2 * KC, KC, 128], fp32, Q + 42048)
    rc8 = sb("rc8", [2 * KC, N], fp32, T + 8192)
    W1s = sb("W1s", [128, KC, 2, H], fp16, Q)
    W2s = sb("W2s", [128, HC, 2, D], fp16, Q + 16384)
    gstage = sb("gstage", [128, 3, 1024], fp32, Q + 32768)
    hTlo = sb("hTlo", [128, HC, N], fp16, Q + 32768)
    ftmp = sb("ftmp", [128, 2, 512], fp32, Q + 52800)
    w1s = sb("w1s", [128, EX * KC * 2 * HE], fp16, Q)
    w2s = sb("w2s", [128, EX * EC * 2 * D], fp16, Q + 24576)
    qf = sb("qf", [128, KC, N], fp32, RR)
    hThi = sb("hThi", [128, HC, N], fp16, RR)
    xe = sb("xe", [B, NB, 2, D], fp16, RR)
    wqst = sb("wqst", [128, KC, 3 * D], fp32, S)
    kv = sb("kv", [B, 2, 2, 2, D], fp16, S + 24576)
    xnt = sb("xnt", [B, 2, D], fp32, S + 32768)
    xhl = sb("xhl", [B, 2, 2, D], fp16, S + 36864)
    wost = sb("wost", [128, KC, D], fp32, S)
    cxt = sb("cxt", [128, KC, 128], fp32, T)
    cxs = sb("cxs", [128, KC, 2, 128], fp16, T + 2048)
    qq = sb("qq", [128, KC, 2, N], fp16, S)
    dbc = sb("dbc", [128, N], fp32, RR)
    diag = sb("diag", [B, NB, B], fp32, S)
    xgt = sb("xgt", [B, 2, D], fp32, S + 8192)
    y1T = sb("y1T", [128, KC, 2, N], fp16, S)
    est = sb("est", [128, 5, 1024], fp32, S)
    acc = sb("acc", [B, NB, D], fp32, T)
    ex = sb("ex", [128, 2, 512], fp32, WO)
    kf = sb("kf", [B, 2, D], fp32, WO + 4096)
    wom = sb("wom", [128, KC, 2, D], fp16, WO)
    xm = sb("xm", [B, 2, D], fp32, WO)
    xet = sb("xet", [B, 2, D], fp32, WO + 4096)
    xv = sb("xv", [B, NB, D], fp32, X)
    xg = sb("xg", [B, NB, 2, D], fp16, X)
    h2 = sb("h2", [B, NB, 2, D], fp16, X)
    xmT = sb("xmT", [128, 2, 512], fp32, Q + 49152)
    xs = sb("xs", [TS, 2, 2, D], fp16, PP)
    xsT = sb("xsT", [128, 2, 2 * KC, TS], fp16, PP + 4096)
    hid = sb("hid", [128, 2, EC * TS], fp32, PP + 8192)
    hids = sb("hids", [128, 2, 2, EC * TS], fp16, PP + 10240)
    yv = sb("yv", [TS, 2, D], fp32, PP + 12288)
    gat = sb("gat", [B, NB, D], fp32, PP + 16384)

    colb = misc("colb", [B, B], i16)
    idh = misc("idh", [128, 128], fp16)
    idf = misc("idf", [128, 128], fp32)
    onf = misc("onf", [B, 128], fp32)
    onh = misc("onh", [B, 128], fp16)
    zeh = misc("zeh", [B, 128], fp16)
    tri = misc("tri", [B, B], fp16)
    mbd = misc("mbd", [128, 128], fp32)
    key = misc("key", [B, ET], fp32)
    srb = misc("srb", [B, ET], fp32)
    b64 = misc("b64", [128, HC], fp32)
    bcur = misc("bcur", [128, 2], fp32)
    large = misc("large", [B, 1], fp16)
    dmax = misc("dmax", [B, 1], fp32)
    code = misc("code", [B, NB, EX], fp32)
    tnum = misc("tnum", [B, EX, NB], fp32)
    oh16 = misc("oh16", [B, NB * EX], fp16)
    bia = misc("bia", [B, D], fp32)
    wgs = misc("wgs", [128, KC, EX], fp32)
    b1s = misc("b1s", [128, HC], fp32)
    gam = misc("gam", [128, KC], fp32)
    gm64 = misc("gm64", [128, KC], fp32)
    negw = misc("negw", [B, NB], fp32)
    tix = misc("tix", [80, 4], fp32)
    iow = misc("iow", [80, NT], fp32)
    tab = misc("tab", [1, 128], i32)
    flg = misc("flg", [1, 4], i32)
    st = misc("st", [B, NB, 6], fp32)
    mv = misc("mv", [B, NB, 2], fp32)
    rs = misc("rs", [B, NB], fp32)
    rs64 = misc("rs64", [B, NB], fp32)
    dinv = misc("dinv", [B, NB], fp32)
    dv64 = misc("dv64", [B, NB], fp32)
    rc = misc("rc", [B, NB], fp32)
    sm = misc("sm", [B, 2, 24], fp32)
    lg = misc("lg", [B, NB, EX], fp32)
    gate = misc("gate", [B, NB], fp32)
    slot = misc("slot", [B, NB], i32)
    eid = misc("eid", [1, 16], i32)
    zrow = sb("zrow", [128, 2 * D], fp16, PP + 44640)
    i_dt = sb("i_dt", [80, 2, B], i32, PP + 46720)
    i_de = sb("i_de", [B, ET], i32, PP + 46720 + 1024)
    i_se = sb("i_se", [B, ET], i32, PP + 46720 + 1664)
    bst = sb("bst", [B, D], fp32, Q + 40000)
    ksum = sb("ksum", [128, KC, 2 * KC], fp32, T + 4096)
    E0 = Q + 51456
    f_dt = sb("f_dt", [80, 2, B], fp32, E0)
    f_mm = sb("f_mm", [80, 2, 2], fp32, E0 + 1024)
    f_in = sb("f_in", [80, 3, 2, NB], fp32, E0 + 1088)
    f_g = sb("f_g", [80, 2, 2, NB], fp32, E0 + 2336)
    f_e = sb("f_e", [NB, 8], fp32, E0 + 3200)
    f_tri = sb("f_tri", [NB, NB + 6], fp32, E0 + 3264)
    f_s = sb("f_s", [B, 3, ET], fp32, E0 + 3584)
    rt = sb("rt", [B, 16, NB, EX], fp32, WO)

    bank = [nc.alloc_psum_tensor(f"bank{b}", [128, 512], fp32) for b in range(8)]
    hbank = [bank[b][:, :].bitcast(fp16) for b in range(8)]

    uses = [1] * 8
    signals = [1] * 8
    first, told = {}, {}

    def claim(stage, counts, signalled=True):
        for b, n in counts.items():
            first[stage, b], told[stage, b] = uses[b], signals[b]
            uses[b] += n
            signals[b] += n * signalled

    SETS = [(0, 1, 2), (3, 6, 7)]
    claim("xT", {0: P2, 1: P2})
    claim("rng", {7: 1, 6: 1})
    claim("kv", {0: P2, 1: P2, 2: P2, 3: P2})
    claim("ctx", {4: 1, 5: 1})
    claim("q", {b: 2 for s in SETS for b in s})
    claim("heads", {0: 1, 1: 1, 2: 1})
    claim("M", {4: 2, 5: 2})
    claim("den", {b: 2 for s in SETS for b in s})
    claim("win", {b: P2 for s in SETS for b in s})
    claim("mix", {4: P2, 5: P2})
    claim("deg", {7: 1, 5: 1})
    claim("dbc", {0: 1, 1: 1, 2: 1})
    claim("l1", {b: 2 for s in SETS for b in s})
    claim("w1", {b: 4 for s in SETS for b in s})
    claim("w2", {4: P2, 5: P2})
    claim("l2", {0: P2, 1: P2})
    claim("xmT", {2: P2, 3: P2})
    claim("gate", {6: P2, 7: P2})
    claim("route", {4: 1, 5: 1})
    claim("xs", {0: NT // 2, 1: NT // 2})
    claim("hid", {2: NT // 2, 3: NT // 2})
    claim("yo", {6: NT // 2, 7: NT // 2})

    ctx = ExitStack()
    with ctx:
        def sem(name):
            return ctx.enter_context(nc.semaphore(name))

        full = [sem(f"bank{b}_written") for b in range(8)]
        free = [sem(f"bank{b}_read") for b in range(8)]

        def can_write(pe, stage, b, k=0):
            pe.wait_ge(free[b], first[stage, b] + k)

        def is_full(eng, stage, b, k=0):
            eng.wait_ge(full[b], k + (told[stage, b] + 1))

        def was_read(eng, stage, b, k=0):
            eng.wait_ge(free[b], k + (first[stage, b] + 1))

        x_in = [sem("x_in0"), sem("x_in1")]
        dt_in, de_in, se_in = sem("dst_tiles_in"), sem("dst_in"), sem("src_in")
        wq_in = [sem(f"wqkv_in{c}") for c in range(KC)]
        small_in, wo_in, bia_in = sem("small_in"), sem("wout_in"), sem("bias_in")
        g_in = [sem(f"gcn_weight_in{b}") for b in range(3)]
        e_in = [sem(f"expert_in{b}") for b in range(5)]
        consts = sem("constants")
        cst0, sel_half = sem("constants_cleared"), sem("heads_one_sided")
        bias_added = sem("bias_added")
        rc1, rs1 = sem("var_reciprocal"), sem("rstd")
        xn_ready, xhi_ready, xlo_ready = ([sem(f"{n}{u}") for u in range(2)] for n in ("xn", "xn_hi", "xn_lo"))
        wqhi, wqlo = sem("wqkv_hi"), sem("wqkv_lo")
        dsteps, asteps, psteps = sem("vector_step"), sem("scalar_step"), sem("gpsimd_step")
        ranges, counts = sem("tile_ranges"), sem("window_counts")
        kf_ready, khi, klo, vhi = ([sem(f"{n}{u}") for u in range(2)] for n in ("kf", "k_hi", "k_lo", "v_hi"))
        ctx_used = [sem("kv_used0"), sem("kv_used1")]
        onehots = sem("source_onehots")
        eq_free = [sem("exp_q_used0"), sem("exp_q_used1")]
        wohi, wolo = sem("wout_hi"), sem("wout_lo")
        cxhi, cxlo = sem("context_hi"), sem("context_lo")
        mhi, qn_ready, qhi = sem("M_hi"), sem("q_scaled"), sem("q_hi")
        keyed, slots_free, chi = sem("tile_keyed"), sem("ring_slots"), sem("counts_hi")
        deg_rc, dinv_r, diag_r, ind_r = (sem(n) for n in ("deg_reciprocal", "dinv", "diag", "large"))
        xg_t, xg_h, xg_l = ([sem(f"{n}{u}") for u in range(2)] for n in ("xg_t", "xg_hi", "xg_lo"))
        ghi, glo = sem("gcn_weight_hi"), sem("gcn_weight_lo")
        y_h, y_l = ([sem(f"{n}{u}") for u in range(2)] for n in ("y_hi", "y_lo"))
        h_h, h_l = ([sem(f"{n}{u}") for u in range(2)] for n in ("h_hi", "h_lo"))
        h2hi = [sem("h2_hi0"), sem("h2_hi1")]
        gms = sem("gamma_scaled")
        ehi, elo = sem("expert_hi"), sem("expert_lo")
        var_r, rstd_r = ([sem(f"{n}{u}") for u in range(2)] for n in ("var", "rstd_block"))
        xm_r = [sem("xm0"), sem("xm1")]
        xe_r, xe_h = ([sem(f"{n}{u}") for u in range(2)] for n in ("xe_t", "xe_hi"))
        xe_done = sem("xe_lo")
        exps_in, exps_out = sem("logits_shifted"), sem("exp_logits")
        picked, slot_r, eid_r = sem("expert_picked"), sem("slots_known"), sem("tile_experts")
        cleared, scattered = sem("slots_cleared"), sem("rows_scattered")
        gathered = [sem(f"rows_gathered{i}") for i in range(NB)]
        zrow_r = sem("zero_rows")
        xs_in = [sem("tile_in0"), sem("tile_in1")]
        hid_h, hid_l = ([sem(f"{n}{u}") for u in range(2)] for n in ("hid_hi", "hid_lo"))
        y_out = [sem("y_out0"), sem("y_out1")]
        fin, stored = sem("final"), sem("stored")

        block = ctx.enter_context(nc.Block())
        HALVES = ((0, 112), (112, B))

        @block.sync
        def _(sp):
            xh = x_d.rearrange("(t p) f -> p t f", p=B)
            for h in range(2):
                for a, b in HALVES:
                    sp.dma_start(xv[a:b, 5 * h:5 * h + 5, :], xh[a:b, 5 * h:5 * h + 5, :]).then_inc(x_in[h], 16)
            sp.dma_start(i_dt[:, :, :], dstt_d.rearrange("(r p) e -> p r e", p=80)).then_inc(dt_in, 16)
            sp.dma_start(i_de[:, :], dst_d).then_inc(de_in, 16)
            sp.dma_start(i_se[:, :], src_d).then_inc(se_in, 16)
            wq = wqkv_d.rearrange("(c p) n -> p c n", p=128)
            for c in range(KC):
                sp.dma_start(wqst[:, c, :], wq[:, c, :]).then_inc(wq_in[c], 16)
            sp.dma_start(wgs[:, :, :], wg_d.rearrange("(c p) e -> p c e", p=128)).then_inc(small_in, 16)
            sp.dma_start(b1s[:, :], b1_d).then_inc(small_in, 16)
            sp.dma_start(gam[:, :], gamma_d).then_inc(small_in, 16)
            sp.wait_ge(zrow_r, 1)
            sp.dma_start(slots_d.rearrange("(k p) d -> p k d", p=TS),
                         zrow[:, :].rearrange("p (a d) -> p a d", a=1).to_broadcast([TS, NT, 2 * D]))\
                .then_inc(cleared, 16)
            sp.wait_ge(wqlo, KC)
            sp.wait_ge(wqhi, KC)
            sp.dma_start(wost[:, :, :], wout_d.rearrange("(c p) n -> p c n", p=128)).then_inc(wo_in, 16)
            for s in SETS:
                for b in s:
                    was_read(sp, "win", b, P2 - 1)
            sp.wait_ge(psteps, 1)
            gw = [W1_d.rearrange("(c p) n -> p c n", p=128)[:, c, :] for c in range(KC)]
            gw += [W2_d.rearrange("(c p) n -> p c n", p=128)[:, 2 * c:2 * c + 2, :] for c in range(HC // 2)]
            for n, w in enumerate(gw):
                if n >= 3:
                    sp.wait_ge(glo, n - 2)
                    sp.wait_ge(ghi, n - 2)
                dst = gstage[:, n % 3, :] if n < KC else gstage[:, n % 3, :].rearrange("p (c n) -> p c n", c=2)
                sp.dma_start(dst, w).then_inc(g_in[n % 3], 16)
            for s in SETS:
                for b in s:
                    is_full(sp, "w1", b, 3)
            v1 = w1_d.rearrange("e (c p) h -> p e c h", p=128)
            v2 = w2_d.rearrange("e (c p) d -> p e c d", p=128)
            for n in range(2 * EX):
                if n >= 5:
                    sp.wait_ge(elo, n - 4)
                    sp.wait_ge(ehi, n - 4)
                w = v1[:, n, :, :] if n < EX else v2[:, n - EX, :, :]
                sp.dma_start(est[:, n % 5, :].rearrange("p (c n) -> p c n", c=KC if n < EX else EC), w)\
                    .then_inc(e_in[n % 5], 16)
            sp.wait_ge(scattered, 16 * NB)
            with sp.Fori(0, NT // 2) as k:
                for u in range(2):
                    sp.wait_ge(full[u], k + told["xs", u])
                    sp.dma_start(xs[:, u, :, :].rearrange("p a d -> p (a d)"),
                                 slots_d[ds(k * (2 * TS) + u * TS, TS), :]).then_inc(xs_in[u], 16)
            oh = out_d.rearrange("(t p) f -> p t f", p=B)
            for h in range(2):
                sp.wait_ge(fin, 5 * h + 5)
                for a, b in HALVES:
                    sp.dma_start(oh[a:b, 5 * h:5 * h + 5, :], acc[a:b, 5 * h:5 * h + 5, :]).then_inc(stored, 16)
            sp.wait_ge(stored, 64)

        @block.gpsimd
        def _(pool):
            S_ = Steps(pool, psteps)
            pool.memset(zrow[:, :], 0.0).then_inc(zrow_r, 1)
            for t in (idh, idf, zeh, strip):
                pool.memset(t[:, :], 0.0).then_inc(cst0, 1)
            for t in (onf, onh, tri, mbd, sel):
                pool.memset(t[:, :, :] if t is sel else t[:, :], 1.0).then_inc(cst0, 1)
            pool.memset(f_tri[:, :], 1.0).then_inc(cst0, 1)
            pool.iota(colw[:, :, :], [[N, NB], [1, B]], base=0, channel_multiplier=0).then_inc(consts, 1)
            pool.iota(colb[:, :], [[1, B]], base=0, channel_multiplier=0).then_inc(consts, 1)
            pool.iota(negw[:, :], [[-B, NB]], base=0, channel_multiplier=0,
                      allow_small_or_imprecise_dtypes=True).then_inc(consts, 1)
            pool.iota(iow[:, :], [[1, NT]], base=0, channel_multiplier=0,
                      allow_small_or_imprecise_dtypes=True).then_inc(consts, 1)
            pool.iota(tix[:, 0:2], [[80, 2]], base=1, channel_multiplier=1,
                      allow_small_or_imprecise_dtypes=True).then_inc(consts, 1)
            pool.iota(tix[:, 2:4], [[-80, 2]], base=256, channel_multiplier=-1,
                      allow_small_or_imprecise_dtypes=True).then_inc(consts, 1)
            pool.wait_ge(cst0, 10)
            for t, n in ((idh, 128), (idf, 128)):
                pool.affine_select(out=t[:, :], in_=t[:, :], compare_op=ALU.not_equal, fill=1.0, base=0,
                                   pattern=[[-1, n]], channel_multiplier=1).then_inc(consts, 1)
            pool.affine_select(out=tri[:, :], in_=tri[:, :], compare_op=ALU.is_gt, fill=0.0, base=0,
                               pattern=[[1, B]], channel_multiplier=-1).then_inc(consts, 1)
            pool.affine_select(out=f_tri[:, :], in_=f_tri[:, :], compare_op=ALU.is_gt, fill=0.0, base=0,
                               pattern=[[1, NB + 6]], channel_multiplier=-1).then_inc(consts, 1)
            v = mbd[:, 0:DH]
            pool.affine_select(out=v, in_=v, compare_op=ALU.is_gt, fill=0.0, base=DH,
                               pattern=[[0, DH]], channel_multiplier=-1).then_inc(consts, 1)
            v = mbd[:, DH:128]
            pool.affine_select(out=v, in_=v, compare_op=ALU.is_ge, fill=0.0, base=-DH,
                               pattern=[[0, DH]], channel_multiplier=1).then_inc(consts, 1)
            pool.affine_select(out=strip[:, N - B:N], in_=strip[:, N - B:N], compare_op=ALU.not_equal, fill=1.0,
                               base=0, pattern=[[-1, B]], channel_multiplier=1).then_inc(consts, 1)
            pool.affine_select(out=sel[:, :, :], in_=sel[:, :, :], compare_op=ALU.is_ge, fill=0.0, base=0,
                               pattern=[[128, KC], [1, 128]], channel_multiplier=-DH).then_inc(sel_half, 1)
            pool.wait_ge(sel_half, 1)
            pool.affine_select(out=sel[:, :, :], in_=sel[:, :, :], compare_op=ALU.is_ge, fill=0.0, base=DH - 1,
                               pattern=[[-128, KC], [-1, 128]], channel_multiplier=DH).then_inc(consts, 1)
            b2row = b2_d.rearrange("(a n) -> a n", a=1).to_broadcast([B, D])
            borow = bout_d.rearrange("(a n) -> a n", a=1).to_broadcast([B, D])
            pool.dma_start(bia[:, :], b2row).then_inc(bia_in, 16)
            pool.dma_start(bst[:, :], borow).then_inc(bia_in, 16)
            pool.iota(code[:, :, :], [[0, NB], [-1, EX]], base=EX, channel_multiplier=0,
                      allow_small_or_imprecise_dtypes=True)
            pool.iota(tnum[:, :, :], [[0, EX], [1, NB]], base=0, channel_multiplier=0,
                      allow_small_or_imprecise_dtypes=True).then_inc(consts, 1)
            pool.wait_ge(bia_in, 32)
            S_.link(pool.tensor_tensor(out=bia[:, :], in0=bia[:, :], in1=bst[:, :], op=ALU.add))
            with pool.Fori(0, P2) as i:
                for u in range(2):
                    was_read(pool, "mix", 4 + u, i)
                    a = acc[:, ds(i * 2 + u, 1), :]
                    pool.tensor_tensor(out=a, in0=a, in1=bia[:, :].rearrange("p (a n) -> p a n", a=1), op=ALU.add)\
                        .then_inc(bias_added, 1)
            for n in range(2 * EX):
                pool.wait_ge(ehi, n + 1)
                if n < EX:
                    o = n * KC * 2 * HE
                    w = w1s[:, o:o + KC * 2 * HE].rearrange("p (c h n) -> p c h n", c=KC, h=2)
                    f = est[:, n % 5, :].rearrange("p (c n) -> p c n", c=KC)
                else:
                    o = (n - EX) * EC * 2 * D
                    w = w2s[:, o:o + EC * 2 * D].rearrange("p (c h n) -> p c h n", c=EC, h=2)
                    f = est[:, n % 5, :].rearrange("p (c n) -> p c n", c=EC)
                pool.tensor_tensor(out=w[:, :, 1, :], in0=f, in1=w[:, :, 0, :], op=ALU.subtract).then_inc(elo, 1)
            pool.wait_ge(cleared, 16)
            pool.wait_ge(slot_r, 1)
            pool.wait_ge(xe_done, NB)
            for u in range(2):
                pool.wait_ge(xe_h[u], P2)
            for i in range(NB):
                pool.indirect_dma_start(
                    out=slots_d[:, :], out_offset=bass.IndirectOffsetOnAxis(ap=slot[:, i:i + 1], axis=0),
                    in_=xe[:, i, :, :].rearrange("p a d -> p (a d)"), in_offset=None).then_inc(scattered, 16)
            for u in range(2):
                pool.wait_ge(y_out[u], 16 * (NT // 2) + 16)
            for i in range(NB):
                pool.indirect_dma_start(
                    out=gat[:, i, :], out_offset=None, in_=yslots_d[:, :],
                    in_offset=bass.IndirectOffsetOnAxis(ap=slot[:, i:i + 1], axis=0)).then_inc(gathered[i], 16)

        @block.tensor
        def _(pe):
            for b in range(8):
                pe.sem_inc(full[b], 1)
                pe.sem_inc(free[b], 1)
            for u in range(2):
                pe.sem_inc(ctx_used[u], 1)
            def split_mm(out, lhs, rhs, start, stop, **kw):
                for n, (a, b) in enumerate(((0, 0), (0, 1), (1, 0))):
                    last = pe.matmul(out, lhs(a), rhs(b), start=start and n == 0, stop=stop and n == 2, **kw)
                return last

            pe.wait_ge(consts, 7)
            with pe.Fori(0, P2) as k:
                for u in range(2):
                    pe.wait_ge(xhi_ready[u], k + 1)
                    pe.wait_ge(xlo_ready[u], k + 2)
                    can_write(pe, "xT", u, k)
                    for c in range(KC):
                        for p in range(2):
                            last = pe.transpose(hbank[u][:, 128 * (2 * c + p):128 * (2 * c + p) + B],
                                                xhl[:, u, p, 128 * c:128 * c + 128], idh[0:B, 0:B])
                    last.then_inc(full[u], 1)

            pe.wait_ge(wqhi, KC)
            pe.wait_ge(wqlo, KC)
            for u in range(2):
                was_read(pe, "xT", u, P2 - 1)

            def kv_block(k, u):
                for z in range(2):
                    b = 2 * u + z
                    can_write(pe, "kv", b, k)
                    for c in range(KC):
                        last = split_mm(bank[b][0:B, :],
                                        lambda p: xnT[:, c, p, ds(k * (2 * B) + u * B, B)],
                                        lambda p: wqkv[:, c, p, D + z * D:2 * D + z * D],
                                        c == 0, c == KC - 1)
                    last.then_inc(full[b], 1)

            def ctx_block(k, u):
                pe.wait_ge(khi[u], k + 1)
                pe.wait_ge(klo[u], k + 2)
                pe.wait_ge(vhi[u], k + 1)
                was_read(pe, "kv", 2 * u + 1, k)
                for p in range(KC):
                    cols = slice(128 * p, 128 * p + 128)
                    split_mm(bank[4][:, cols], lambda h: kv[:, u, 1, h, cols], lambda h: kv[:, u, 0, h, cols],
                             False, False, skip_group_check=True)
                    for h in range(2):
                        last = pe.matmul(bank[5][:, p:p + 1], kv[:, u, 0, h, cols], onh[:, 0:1],
                                         start=False, stop=False, skip_group_check=True)
                last.then_inc(ctx_used[u], 1)

            pe.wait_ge(consts, 14)
            for b in (4, 5):
                pe.matmul(bank[b][:, 0:1], zeh[:, :], zeh[:, 0:1], start=True, stop=False, skip_group_check=True)
            kv_block(0, 0)
            pe.wait_ge(ranges, 1)
            for n in range(4):
                last = pe.transpose(bank[7][0:NB, 80 * n:80 * n + 80],
                                    f_g[:, n // 2, n % 2, :], idf[0:80, 0:80])
            last.then_inc(full[7], 1)
            pe.wait_ge(counts, 1)
            pe.matmul(bank[6][0:1, 0:NB + 1], f_e[:, 2:3], f_tri[:, 0:NB + 1], start=True, stop=True)
            pe.matmul(bank[6][0:1, 64:64 + NB], f_e[:, 3:4], idf[0:NB, 0:NB], start=True, stop=True)\
                .then_inc(full[6], 1)
            with pe.Fori(0, P2 - 1) as k:
                kv_block(k, 1)
                ctx_block(k, 0)
                kv_block(k + 1, 0)
                ctx_block(k, 1)
            kv_block(P2 - 1, 1)
            ctx_block(P2 - 1, 0)
            def q_rows(k, u):
                for (a, n), b in zip(CH, SETS[u]):
                    can_write(pe, "q", b, k)
                    for c in range(KC):
                        last = split_mm(bank[b][:, 0:n], lambda p: wqkv[:, c, p, ds(k * 256 + u * 128, 128)],
                                        lambda p: xnT[:, c, p, a:a + n], c == 0, c == KC - 1)
                    last.then_inc(full[b], 1)

            q_rows(0, 0)
            ctx_block(P2 - 1, 1)
            for b in (4, 5):
                pe.matmul(bank[b][:, 0:1], zeh[:, :], zeh[:, 0:1], start=False, stop=True,
                          skip_group_check=True).then_inc(full[b], 1)
            q_rows(0, 1)
            q_rows(1, 0)
            q_rows(1, 1)
            was_read(pe, "ctx", 5)
            for m in range(2):
                pe.wait_ge(eq_free[m], 7)
            for b, (a, m) in enumerate(CH):
                can_write(pe, "heads", b)
                for p in range(KC):
                    last = pe.matmul(bank[b][0:2 * KC, 0:m], ksum[:, p, :], qf[:, p, a:a + m],
                                     start=(p == 0), stop=(p == KC - 1))
                last.then_inc(full[b], 1)
            pe.wait_ge(wohi, 1)
            pe.wait_ge(wolo, 1)
            pe.wait_ge(cxhi, 1)
            pe.wait_ge(cxlo, 1)
            for p in range(KC):
                b = 4 + p % 2
                can_write(pe, "M", b, p // 2)
                split_mm(bank[b][:, :], lambda h: cxs[:, p, h, :], lambda h: wom[:, p, h, :], True, True)\
                    .then_inc(full[b], 1)
            for p in range(KC):
                for n, ((a, m), b) in enumerate(zip(CH, SETS[p % 2])):
                    if p == 0:
                        was_read(pe, "heads", n)
                    can_write(pe, "den", b, p // 2)
                    pe.matmul(bank[b][:, 0:m], sel[:, p, :], rc8[:, a:a + m], start=True, stop=True)\
                        .then_inc(full[b], 1)
            pe.wait_ge(onehots, NB)
            was_read(pe, "rng", 6)

            def window(a, k, u):
                s0 = pe.value_load(tab[0:1, ds(a, 1)], min_val=0, max_val=NB * ET)
                s1 = pe.value_load(tab[0:1, ds(a + 1, 1)], min_val=0, max_val=NB * ET)
                b0 = pe.value_load(tab[0:1, ds(a + 64, 1)], min_val=0, max_val=ET - TT)
                for (f, c), b in zip(WIN, SETS[u]):
                    can_write(pe, "win", b, k)
                    pe.matmul(bank[b][0:B, 0:c * B], idh[0:B, 0:B], strip[:, ds(a * -B + (N - B + f * B), c * B)],
                              start=True, stop=False, skip_group_check=True)
                with pe.Fori(s0, s1) as n:
                    t = ((n - s0) * TT + b0).with_bounds(min_val=0, max_val=ET - TT)
                    pe.wait_ge(keyed, n + 1)
                    ones, dests = oneb[:, ds(t * B, TT * B)], ring[:, ds((n % R) * (TT * N), TT * N)]
                    for v in range(TT):
                        for (f, c), b in zip(WIN, SETS[u]):
                            last = pe.matmul(bank[b][0:B, 0:c * B], ones[:, v * B:v * B + B],
                                             dests[:, v * N + f * B:v * N + (f + c) * B],
                                             start=False, stop=False, skip_group_check=True)
                    last.then_inc(slots_free, 1)
                for (f, c), b in zip(WIN, SETS[u]):
                    pe.matmul(bank[b][0:B, 0:1], zeh[0:B, 0:B], zeh[0:B, 0:1], start=False, stop=True,
                              skip_group_check=True).then_inc(full[b], 1)

            def mix(a, k, u):
                can_write(pe, "mix", 4 + u, k)
                for p in range(KC):
                    last = split_mm(bank[4 + u][0:B, :], lambda h: qq[:, p, h, ds(a * B, B)],
                                    lambda h: wom[:, p, h, :], p == 0, p == KC - 1)
                last.then_inc(full[4 + u], 1)

            for b in (4, 5):
                was_read(pe, "M", b, 1)
            for s in SETS:
                for b in s:
                    was_read(pe, "den", b, 1)
            with pe.Fori(0, P2) as k:
                for u in range(2):
                    window(k * 2 + u, k, u)
                    mix(k * 2 + u, k, u)
            for s in SETS:
                for b in s:
                    was_read(pe, "win", b, P2 - 1)
            can_write(pe, "deg", 7)
            def degree(i):
                for a in range(NB):
                    for h, C in enumerate((Chi, Clo)):
                        last = pe.matmul(bank[7][0:B, ds(i, 1)], C[:, a, ds(i * B, B)], onh[:, 0:1],
                                         start=(a == 0 and h == 0), stop=(a == NB - 1 and h == 1))
                return last

            with pe.Fori(0, NB - 1) as i:
                degree(i)
            degree(NB - 1).then_inc(full[7], 1)
            can_write(pe, "deg", 5)
            pe.wait_ge(ind_r, 1)
            pe.matmul(bank[5][0:1, 0:1], large[:, 0:1], onh[:, 0:1], start=True, stop=True).then_inc(full[5], 1)
            pe.wait_ge(diag_r, 1)
            for i in range(NB):
                b, o = i // 4, B * (i % 4)
                if i % 4 == 0:
                    can_write(pe, "dbc", b)
                last = pe.matmul(bank[b][:, o:o + B], onf[:, :], diag[:, i, :], start=True, stop=True)
                if i % 4 == 3 or i == NB - 1:
                    last.then_inc(full[b], 1)
            was_read(pe, "deg", 5)
            some_low = pe.value_load(flg[0:1, 0:1], min_val=0, max_val=1)
            for u in range(2):
                pe.wait_ge(xg_h[u], P2)
                pe.wait_ge(xg_l[u], P2 + 1)
            with pe.Fori(0, 2) as k:
                for u in range(2):
                    for (a, n), b in zip(CH, SETS[u]):
                        can_write(pe, "l1", b, k)
                        cols = ds(k * 256 + u * 128, 128)
                        for s in range(NB - 1):
                            for h in range(2):
                                pe.matmul(bank[b][:, 0:n], xg[:, s, h, cols], Chi[:, s, a:a + n],
                                          start=(s == 0 and h == 0), stop=False)
                        with pe.If(some_low > 0):
                            for s in range(NB):
                                for h in range(2):
                                    pe.matmul(bank[b][:, 0:n], xg[:, s, h, cols], Clo[:, s, a:a + n],
                                              start=False, stop=False)
                        for h in range(2):
                            last = pe.matmul(bank[b][:, 0:n], xg[:, NB - 1, h, cols], Chi[:, NB - 1, a:a + n],
                                             start=False, stop=(h == 1))
                        last.then_inc(full[b], 1)
            pe.wait_ge(ghi, KC)
            pe.wait_ge(glo, KC)
            for u in range(2):
                pe.wait_ge(y_h[u], 6)
                pe.wait_ge(y_l[u], 7)
            with pe.Fori(0, HC // 2) as k:
                for u in range(2):
                    for (a, n), b in zip(CH, SETS[u]):
                        can_write(pe, "w1", b, k)
                        for c in range(KC):
                            last = split_mm(bank[b][:, 0:n], lambda p: W1s[:, c, p, ds(k * 256 + u * 128, 128)],
                                            lambda p: y1T[:, c, p, a:a + n], c == 0, c == KC - 1)
                        last.then_inc(full[b], 1)
            pe.wait_ge(ghi, KC + HC // 2)
            pe.wait_ge(glo, KC + HC // 2)
            for u in range(2):
                pe.wait_ge(h_h[u], 12)
                pe.wait_ge(h_l[u], 13)
            hT = (hThi, hTlo)
            with pe.Fori(0, P2) as k:
                for u in range(2):
                    b = 4 + u
                    can_write(pe, "w2", b, k)
                    for c in range(HC):
                        last = split_mm(bank[b][0:B, :], lambda p: hT[p][:, c, ds(k * (2 * B) + u * B, B)],
                                        lambda p: W2s[:, c, p, :], c == 0, c == HC - 1)
                    last.then_inc(full[b], 1)
            for u in range(2):
                was_read(pe, "w2", 4 + u, P2 - 1)
                pe.wait_ge(h2hi[u], P2)
            pe.wait_ge(small_in, 48)

            def agg(k, u):
                can_write(pe, "l2", u, k)
                for s in range(NB - 1):
                    for h in range(2):
                        pe.matmul(bank[u][0:B, :], Chi[:, s, ds(k * (2 * B) + u * B, B)], h2[:, s, h, :],
                                  start=(s == 0 and h == 0), stop=False)
                with pe.If(some_low > 0):
                    for s in range(NB):
                        for h in range(2):
                            pe.matmul(bank[u][0:B, :], Clo[:, s, ds(k * (2 * B) + u * B, B)], h2[:, s, h, :],
                                      start=False, stop=False)
                for h in range(2):
                    last = pe.matmul(bank[u][0:B, :], Chi[:, NB - 1, ds(k * (2 * B) + u * B, B)],
                                     h2[:, NB - 1, h, :], start=False, stop=(h == 1))
                last.then_inc(full[u], 1)

            def logits(k, u):
                pe.wait_ge(xm_r[u], k + 1)
                can_write(pe, "xmT", 2 + u, k)
                for c in range(KC):
                    last = pe.transpose(bank[2 + u][:, 128 * c:128 * c + B], xm[:, u, 128 * c:128 * c + 128],
                                        idf[0:B, 0:B])
                last.then_inc(full[2 + u], 1)
                was_read(pe, "xmT", 2 + u, k)
                can_write(pe, "gate", 6 + u, k)
                for c in range(KC):
                    last = pe.matmul(bank[6 + u][0:B, 0:EX], xmT[:, u, 128 * c:128 * c + B], wgs[:, c, :],
                                     start=(c == 0), stop=(c == KC - 1))
                last.then_inc(full[6 + u], 1)

            agg(0, 0)
            with pe.Fori(0, P2 - 1) as k:
                agg(k, 1)
                logits(k, 0)
                agg(k + 1, 0)
                logits(k, 1)
            agg(P2 - 1, 1)
            logits(P2 - 1, 0)
            logits(P2 - 1, 1)
            pe.wait_ge(picked, 1)
            can_write(pe, "route", 4)
            pe.matmul(bank[4][0:B, 0:NB * EX], tri[:, :], oh16[:, :], start=True, stop=True)
            pe.matmul(bank[4][0:B, 64:64 + NB * EX], onh[:, 0:B], oh16[:, :], start=True, stop=True)\
                .then_inc(full[4], 1)
            pe.wait_ge(eid_r, 1)
            pe.wait_ge(ehi, 2 * EX)
            pe.wait_ge(elo, 2 * EX)

            def load_T(k, u):
                pe.wait_ge(xs_in[u], k * 16 + 16)
                can_write(pe, "xs", u, k)
                for c in range(KC):
                    for p in range(2):
                        last = pe.transpose(hbank[u][:, 128 * (2 * c + p):128 * (2 * c + p) + TS],
                                            xs[:, u, p, 128 * c:128 * c + 128], idh[:, :])
                last.then_inc(full[u], 1)

            def expert(k, u):
                e = pe.value_load(eid[0:1, ds(k * 2 + u, 1)], min_val=0, max_val=EX - 1)
                was_read(pe, "xs", u, k)
                can_write(pe, "hid", 2 + u, k)
                for j in range(EC):
                    for c in range(KC):
                        last = split_mm(bank[2 + u][:, TS * j:TS * j + TS],
                                        lambda p: w1s[:, ds(e * (KC * 2 * HE) + (2 * c + p) * HE + 128 * j, 128)],
                                        lambda p: xsT[:, u, 2 * c + p, :], c == 0, c == KC - 1)
                last.then_inc(full[2 + u], 1)
                return e

            def expert_out(k, u, e):
                pe.wait_ge(hid_h[u], k + 1)
                pe.wait_ge(hid_l[u], k + 2)
                can_write(pe, "yo", 6 + u, k)
                for j in range(EC):
                    last = split_mm(bank[6 + u][:, :], lambda p: hids[:, u, p, TS * j:TS * j + TS],
                                    lambda p: w2s[:, ds(e * (EC * 2 * D) + (2 * j + p) * D, D)],
                                    j == 0, j == EC - 1)
                last.then_inc(full[6 + u], 1)

            def pair(k, more):
                e0 = expert(k, 0)
                e1 = expert(k, 1)
                if more:
                    load_T(k + 1, 0)
                    load_T(k + 1, 1)
                expert_out(k, 0, e0)
                expert_out(k, 1, e1)

            load_T(0, 0)
            load_T(0, 1)
            with pe.Fori(0, NT // 2 - 1) as k:
                pair(k, True)
            pair(NT // 2 - 1, False)

        @block.scalar
        def _(act):
            S_ = Steps(act, asteps)
            for u in range(2):
                act.sem_inc(y_out[u], 16)
            act.wait_ge(rc1, 1)
            act.activation(rs[:, :], rc[:, :], ACT.Sqrt).then_inc(rs1, 1)
            with act.Fori(0, P2) as k:
                for u in range(2):
                    act.wait_ge(xn_ready[u], k + 1)
                    act.activation(xhl[:, u, 0, :], xnt[:, u, :], ACT.Copy).then_inc(xhi_ready[u], 1)
                for u in range(2):
                    is_full(act, "xT", u, k)
                    act.activation(xnT[:, :, :, ds(k * (2 * B) + u * B, B)].rearrange("p c h n -> p (c h) n"),
                                   hbank[u][:, :].rearrange("p (c n) -> p c n", n=128)[:, :, 0:B], ACT.Copy)\
                        .then_inc(free[u], 1)
            for c in range(KC):
                act.wait_ge(wq_in[c], 16)
                act.activation(wqkv[:, c, 0, :], wqst[:, c, :], ACT.Copy, scale=S6).then_inc(wqhi, 1)
            def k_block(k, u):
                act.wait_ge(klo[u], k + 1)
                is_full(act, "kv", 2 * u, k)
                act.activation(ex[0:B, u, :], bank[2 * u][0:B, :], ACT.Exp, scale=UN)
                act.activation(kf[:, u, :], bank[2 * u][0:B, :], ACT.Relu, scale=UN).then_inc(free[2 * u], 1)
                is_full(act, "kv", 2 * u + 1, k)
                act.wait_ge(ctx_used[u], k + 1)
                act.activation(kv[:, u, 1, 0, :], bank[2 * u + 1][0:B, :], ACT.Copy, scale=1.0 / S6)\
                    .then_inc(vhi[u], 1)
                act.wait_ge(kf_ready[u], k + 1)
                act.activation(kv[:, u, 0, 0, :], kf[:, u, :], ACT.Copy, scale=S6).then_inc(khi[u], 1)

            with act.Fori(0, P2) as k:
                k_block(k, 0)
                k_block(k, 1)
            for u in range(2):
                act.wait_ge(klo[u], P2 + 1)
            with act.Fori(0, 2) as k:
                for m in range(6):
                    (a, n), b = CH[m % 3], SETS[m // 3][m % 3]
                    is_full(act, "q", b, k)
                    act.wait_ge(eq_free[m % 2], k * 3 + (m // 2 + 1))
                    act.activation(ex[:, m % 2, 0:n], bank[b][:, 0:n], ACT.Exp, scale=UN * QS)
                    act.activation(qf[:, ds(k * 2 + m // 3, 1), a:a + n],
                                   bank[b][:, 0:n].rearrange("p (a n) -> p a n", a=1), ACT.Relu, scale=UN * QS)\
                        .then_inc(free[b], 1)
            act.wait_ge(wo_in, 16)
            for u in range(2):
                act.wait_ge(eq_free[u], 7)
            act.activation(wom[:, :, 0, :], wost[:, :, :], ACT.Copy, scale=S6).then_inc(wohi, 1)
            was_read(act, "ctx", 4)
            act.activation(cxs[:, :, 0, :], cxt[:, :, :], ACT.Copy).then_inc(cxhi, 1)
            for p in range(KC):
                is_full(act, "M", 4 + p % 2, p // 2)
                act.activation(wom[:, p, 0, :], bank[4 + p % 2][:, :], ACT.Copy, scale=1.0 / 16).then_inc(mhi, 1)
            for p in range(KC):
                for n, (a, m) in enumerate(CH):
                    act.wait_ge(qn_ready, 3 * p + n + 1)
                    act.activation(qq[:, p, 0, a:a + m], qf[:, p, a:a + m], ACT.Copy).then_inc(qhi, 1)
            with act.Fori(0, P2) as k:
                for u in range(2):
                    for (f, c), b in zip(WIN, SETS[u]):
                        is_full(act, "win", b, k)
                        act.activation(Chi[:, f:f + c, ds(k * (2 * B) + u * B, B)],
                                       bank[b][0:B, 0:c * B].rearrange("p (a n) -> p a n", n=B), ACT.Copy)\
                            .then_inc(chi, 1)
            act.wait_ge(deg_rc, 1)
            act.activation(dinv[:, :], rc[:, :], ACT.Sqrt).then_inc(dinv_r, 1)
            with act.Fori(0, P2) as k:
                for u in range(2):
                    act.wait_ge(xg_t[u], k + 1)
                    act.activation(xg[:, ds(k * 2 + u, 1), 0, :],
                                   xgt[:, u, :].rearrange("p (a n) -> p a n", a=1), ACT.Copy).then_inc(xg_h[u], 1)
            for b in range(3):
                is_full(act, "dbc", b)
                m = min(4 * B, N - 4 * B * b)
                act.activation(dbc[:, 4 * B * b:4 * B * b + m], bank[b][:, 0:m], ACT.Copy).then_inc(free[b], 1)
            for n in range(KC):
                act.wait_ge(g_in[n % 3], 16 * (n // 3 + 1))
                act.activation(W1s[:, n, 0, :], gstage[:, n % 3, :], ACT.Copy, scale=S6).then_inc(ghi, 1)
            with act.Fori(0, 2) as k:
                for m in range(6):
                    (a, n), b = CH[m % 3], SETS[m // 3][m % 3]
                    was_read(act, "l1", b, k)
                    act.activation(y1T[:, ds(k * 2 + m // 3, 1), 0, a:a + n],
                                   ftmp[:, m % 2, 0:n].rearrange("p (a n) -> p a n", a=1), ACT.Copy)\
                        .then_inc(y_h[m % 2], 1)
            for n in range(KC, KC + HC // 2):
                act.wait_ge(g_in[n % 3], 16 * (n // 3 + 1))
                c = 2 * (n - KC)
                act.activation(W2s[:, c:c + 2, 0, :], gstage[:, n % 3, :].rearrange("p (c n) -> p c n", c=2),
                               ACT.Copy, scale=S6).then_inc(ghi, 1)
            act.wait_ge(small_in, 48)
            S_.link(act.mul(b64[:, :], b1s[:, :], S6))
            for u in range(2):
                act.wait_ge(y_l[u], 7)
            with S_.loop(HC // 2, 2):
                k = S_.i
                for m in range(6):
                    (a, n), b = CH[m % 3], SETS[m // 3][m % 3]
                    if m % 3 == 0:
                        S_.link(act.activation(bcur[:, m // 3:m // 3 + 1], b64[:, ds(k * 2 + m // 3, 1)], ACT.Copy))
                    act.wait_ge(h_l[m % 2], k * 3 + (m // 2 + 1))
                    is_full(act, "w1", b, k)
                    act.activation(ftmp[:, m % 2, 0:n], bank[b][:, 0:n], ACT.Relu, scale=1.0 / S6,
                                   bias=bcur[:, m // 3:m // 3 + 1]).then_inc(free[b], 1)
                    was_read(act, "w1", b, k)
                    act.activation(hThi[:, ds(k * 2 + m // 3, 1), a:a + n],
                                   ftmp[:, m % 2, 0:n].rearrange("p (a n) -> p a n", a=1), ACT.Copy)\
                        .then_inc(h_h[m % 2], 1)
            with act.Fori(0, P2) as k:
                for u in range(2):
                    i = k * 2 + u
                    is_full(act, "w2", 4 + u, k)
                    act.activation(h2[:, ds(i, 1), 0, :], bank[4 + u][0:B, :].rearrange("p (a n) -> p a n", a=1),
                                   ACT.Copy, scale=dv64[:, ds(i, 1)]).then_inc(h2hi[u], 1)
            act.wait_ge(gms, 1)
            for u in range(2):
                is_full(act, "w2", 4 + u, P2 - 1)

            def expert_hi(n):
                act.wait_ge(e_in[n % 5], 16 * (n // 5 + 1))
                f = est[:, n % 5, :].rearrange("p (c n) -> p c n", c=KC if n < EX else EC)
                if n < EX:
                    for c in range(KC):
                        last = act.activation(f[:, c, :], f[:, c, :], ACT.Copy, scale=gm64[:, c:c + 1])
                    o = n * KC * 2 * HE
                    w = w1s[:, o:o + KC * 2 * HE].rearrange("p (c h n) -> p c h n", c=KC, h=2)
                else:
                    last = act.activation(f, f, ACT.Copy, scale=S6)
                    o = (n - EX) * EC * 2 * D
                    w = w2s[:, o:o + EC * 2 * D].rearrange("p (c h n) -> p c h n", c=EC, h=2)
                S_.link(last)
                act.activation(w[:, :, 0, :], f, ACT.Copy).then_inc(ehi, 1)

            for k in range(P2):
                for u in range(2):
                    i = 2 * k + u
                    act.wait_ge(var_r[u], 2 * k + 1)
                    act.activation(sm[:, u, 9:10], sm[:, u, 8:9], ACT.Sqrt).then_inc(rstd_r[u], 1)
                    act.wait_ge(var_r[u], 2 * k + 2)
                    act.activation(sm[:, u, 19:20], sm[:, u, 18:19], ACT.Sqrt, scale=S6 * S6).then_inc(rstd_r[u], 1)
                    act.wait_ge(xe_r[u], k + 1)
                    act.activation(xe[:, i, 0, :], xet[:, u, :], ACT.Copy).then_inc(xe_h[u], 1)
                    is_full(act, "xmT", 2 + u, k)
                    act.activation(xmT[:, u, :].rearrange("p (c n) -> p c n", n=128)[:, :, 0:B],
                                   bank[2 + u][:, :].rearrange("p (c n) -> p c n", n=128)[:, :, 0:B], ACT.Copy)\
                        .then_inc(free[2 + u], 1)
                    expert_hi(i)
            expert_hi(10)
            expert_hi(11)
            act.wait_ge(exps_in, 1)
            act.activation(rt[:, 1, :, :], rt[:, 0, :, :], ACT.Exp).then_inc(exps_out, 1)
            def tile_T(k, u):
                is_full(act, "xs", u, k)
                act.activation(xsT[:, u, :, :], hbank[u][:, :].rearrange("p (c n) -> p c n", n=128), ACT.Copy)\
                    .then_inc(free[u], 1)

            def gelu(k, u):
                is_full(act, "hid", 2 + u, k)
                act.wait_ge(hid_l[u], k + 1)
                act.activation(hid[:, u, :], bank[2 + u][:, 0:EC * TS], ACT.Gelu, scale=UN)\
                    .then_inc(free[2 + u], 1)

            def gelu_hi(k, u):
                was_read(act, "hid", 2 + u, k)
                act.activation(hids[:, u, 0, :], hid[:, u, :], ACT.Copy, scale=S6).then_inc(hid_h[u], 1)

            def y_tile(k, u):
                is_full(act, "yo", 6 + u, k)
                act.wait_ge(y_out[u], k * 16 + 16)
                act.activation(yv[:, u, :], bank[6 + u][:, :], ACT.Copy, scale=UN).then_inc(free[6 + u], 1)
                was_read(act, "yo", 6 + u, k)
                act.dma_start(yslots_d[ds(k * (2 * TS) + u * TS, TS), :], yv[:, u, :]).then_inc(y_out[u], 16)

            def pair_out(k, more):
                for u in range(2):
                    gelu(k, u)
                    gelu_hi(k, u)
                for u in range(2):
                    if more:
                        tile_T(k + 1, u)
                for u in range(2):
                    y_tile(k, u)

            tile_T(0, 0)
            tile_T(0, 1)
            with act.Fori(0, NT // 2 - 1) as k:
                pair_out(k, True)
            pair_out(NT // 2 - 1, False)

        @block.vector
        def _(dve):
            V = Steps(dve, dsteps)
            dve.sem_inc(slots_free, R)
            for s in (xlo_ready, klo, eq_free, xg_l, y_l, h_l, hid_l):
                for u in range(2):
                    dve.sem_inc(s[u], 1)
            for i in range(NB):
                dve.wait_ge(x_in[i // 5], 32)
                last = dve.bn_stats(st[:, i, :], xv[:, i, :])
                V.mark(last)
            V.wait()
            for i in range(NB):
                V.mark(dve.bn_aggr(mv[:, i, :], st[:, i, :]))
            V.wait()
            V.link(dve.tensor_scalar(rc[:, :], mv[:, :, 1], EPS, None, ALU.add))
            dve.reciprocal(rc[:, :], rc[:, :]).then_inc(rc1, 1)
            dve.wait_ge(rs1, 1)
            V.link(dve.tensor_scalar(rs64[:, :], rs[:, :], S6, None, ALU.mult))
            with dve.Fori(0, P2) as k:
                for u in range(2):
                    i = k * 2 + u
                    dve.wait_ge(xlo_ready[u], k + 1)
                    dve.tensor_scalar(xnt[:, u, :], xv[:, ds(i, 1), :].rearrange("p a n -> p (a n)"),
                                      mv[:, ds(i, 1), 0], rs64[:, ds(i, 1)],
                                      ALU.subtract, ALU.mult).then_inc(xn_ready[u], 1)
                for u in range(2):
                    dve.wait_ge(xhi_ready[u], k + 1)
                    dve.wait_ge(full[u], k + told["xT", u])
                    dve.tensor_tensor(xhl[:, u, 1, :], xnt[:, u, :], xhl[:, u, 0, :], ALU.subtract)\
                        .then_inc(xlo_ready[u], 1)
            for c in range(KC):
                dve.wait_ge(wqhi, c + 1)
                dve.scalar_tensor_tensor(wqkv[:, c, 1, :], wqst[:, c, :], S6, wqkv[:, c, 0, :],
                                         ALU.mult, ALU.subtract).then_inc(wqlo, 1)
            dve.wait_ge(consts, 12)
            dve.wait_ge(se_in, 16)
            dve.wait_ge(de_in, 16)
            V.link(dve.tensor_copy(f_s[:, 0, :], i_se[:, :]))
            V.link(dve.tensor_scalar(f_s[:, 1, :], f_s[:, 0, :], 1.0 / B, -0.5 + 0.5 / B, ALU.mult, ALU.add))
            V.link(dve.tensor_scalar(f_s[:, 1, :], f_s[:, 1, :], BIG, BIG, ALU.add, ALU.subtract))
            V.link(dve.tensor_copy(f_s[:, 2, :], i_de[:, :]))
            V.mark(dve.scalar_tensor_tensor(srb[:, :], f_s[:, 1, :], -float(B), f_s[:, 0, :], ALU.mult, ALU.add))
            V.link(dve.scalar_tensor_tensor(key[:, :], f_s[:, 1, :], float(N), f_s[:, 2, :], ALU.mult, ALU.add))
            dve.wait_ge(dt_in, 16)
            V.link(dve.tensor_copy(f_dt[:, :, :], i_dt[:, :, :]))
            V.mark(dve.tensor_reduce(f_mm[:, 0, :], f_dt[:, :, :], AX.X, ALU.min))
            V.link(dve.tensor_reduce(f_mm[:, 1, :], f_dt[:, :, :], AX.X, ALU.max))
            V.link(dve.tensor_scalar(f_mm[:, :, :], f_mm[:, :, :], 1.0 / B, -0.5 + 0.5 / B, ALU.mult, ALU.add))
            V.link(dve.tensor_scalar(f_mm[:, :, :], f_mm[:, :, :], BIG, BIG, ALU.add, ALU.subtract))
            for r in range(2):
                V.mark(dve.tensor_scalar(f_in[:, 2, r, :], iow[:, 0:NB], f_mm[:, 1, r:r + 1], None, ALU.is_le))
                for q in range(2):
                    V.mark(dve.tensor_scalar(f_in[:, q, r, :], iow[:, 0:NB], f_mm[:, 0, r:r + 1],
                                             tix[:, 2 * q + r:2 * q + r + 1], ALU.is_ge, ALU.mult))
            V.wait()
            dve.tensor_tensor(f_g[:, 0, :, :], f_in[:, 0, :, :], f_in[:, 2, :, :], ALU.mult)
            dve.tensor_tensor(f_g[:, 1, :, :], f_in[:, 1, :, :], f_in[:, 2, :, :], ALU.mult).then_inc(ranges, 1)
            is_full(dve, "rng", 7)
            dve.tensor_reduce(f_e[:, 0:2], bank[7][0:NB, 0:320].rearrange("p (q n) -> p q n", q=2), AX.X, ALU.max)\
                .then_inc(free[7], 1)
            was_read(dve, "rng", 7)
            V.mark(dve.tensor_scalar(f_e[:, 4:5], f_e[:, 0:1], 1.0, None, ALU.max))
            V.link(dve.tensor_scalar(f_e[:, 5:6], f_e[:, 1:2], -1.0, 256.0, ALU.mult, ALU.add))
            V.link(dve.tensor_scalar(f_e[:, 6:7], f_e[:, 4:5], 1.0, None, ALU.subtract))
            V.link(dve.tensor_tensor(f_e[:, 3:4], f_e[:, 5:6], f_e[:, 6:7], ALU.min))
            V.link(dve.tensor_tensor(f_e[:, 4:5], f_e[:, 4:5], f_e[:, 3:4], ALU.subtract))
            V.link(dve.tensor_scalar(f_e[:, 4:5], f_e[:, 4:5], 1.0 / TT, 0.5 - 0.5 / TT, ALU.mult, ALU.add))
            V.link(dve.tensor_scalar(f_e[:, 2:3], f_e[:, 4:5], BIG, BIG, ALU.add, ALU.subtract))
            V.link(dve.tensor_scalar(f_e[:, 5:6], f_e[:, 2:3], -float(TT), float(ET), ALU.mult, ALU.add))
            dve.tensor_tensor(f_e[:, 3:4], f_e[:, 3:4], f_e[:, 5:6], ALU.min).then_inc(counts, 1)
            is_full(dve, "rng", 6)
            dve.tensor_copy(tab[0:1, 0:NB + 1], bank[6][0:1, 0:NB + 1])
            dve.tensor_copy(tab[0:1, 64:64 + NB], bank[6][0:1, 64:64 + NB]).then_inc(free[6], 1)
            def k_low(k, u):
                was_read(dve, "kv", 2 * u, k)
                dve.scalar_tensor_tensor(kf[:, u, :], ex[0:B, u, :], 1.0, kf[:, u, :], ALU.min, ALU.add)\
                    .then_inc(kf_ready[u], 1)
                dve.wait_ge(vhi[u], k + 1)
                dve.scalar_tensor_tensor(kv[:, u, 1, 1, :], bank[2 * u + 1][0:B, :], 1.0 / S6, kv[:, u, 1, 0, :],
                                         ALU.mult, ALU.subtract).then_inc(free[2 * u + 1], 1)
                dve.wait_ge(khi[u], k + 1)
                dve.scalar_tensor_tensor(kv[:, u, 0, 1, :], kf[:, u, :], S6, kv[:, u, 0, 0, :],
                                         ALU.mult, ALU.subtract).then_inc(klo[u], 1)

            with dve.Fori(0, P2) as k:
                for u in range(2):
                    k_low(k, u)
                    for s in range(ET // NB):
                        t = k * (2 * ET // NB) + (u * (ET // NB) + s)
                        last = dve.tensor_scalar(oneb[:, ds(t * B, B)], colb[:, :], srb[:, ds(t, 1)], None,
                                                 ALU.is_equal)
                    last.then_inc(onehots, 1)
            is_full(dve, "ctx", 4)
            is_full(dve, "ctx", 5)
            for p in range(KC):
                last = dve.scalar_tensor_tensor(cxt[:, p, :], bank[4][:, 128 * p:128 * p + 128], CXS, mbd[:, :],
                                                ALU.mult, ALU.mult)
            last.then_inc(free[4], 1)
            V.link(dve.memset(ksum[:, :, :], 0.0))
            for p in range(KC):
                last = dve.tensor_scalar(ksum[:, p, 2 * p:2 * p + 2], mbd[:, 0:128:DH], bank[5][:, p:p + 1], BDS,
                                         ALU.mult, ALU.mult)
            last.then_inc(free[5], 1)
            with dve.Fori(0, 2) as k:
                for m in range(6):
                    (a, n), b = CH[m % 3], SETS[m // 3][m % 3]
                    was_read(dve, "q", b, k)
                    q = qf[:, ds(k * 2 + m // 3, 1), a:a + n].rearrange("p a n -> p (a n)")
                    dve.scalar_tensor_tensor(q, ex[:, m % 2, 0:n], 1.0, q, ALU.min, ALU.add)\
                        .then_inc(eq_free[m % 2], 1)
            dve.wait_ge(wohi, 1)
            dve.scalar_tensor_tensor(wom[:, :, 1, :], wost[:, :, :], S6, wom[:, :, 0, :], ALU.mult, ALU.subtract)\
                .then_inc(wolo, 1)
            dve.wait_ge(cxhi, 1)
            dve.tensor_tensor(cxs[:, :, 1, :], cxt[:, :, :], cxs[:, :, 0, :], ALU.subtract).then_inc(cxlo, 1)
            for b, (a, m) in enumerate(CH):
                is_full(dve, "heads", b)
                V.link(dve.tensor_scalar(rc8[:, a:a + m], bank[b][0:2 * KC, 0:m], 1e-8 / (N * 1024.0), None, ALU.add))
                dve.reciprocal(rc8[:, a:a + m], rc8[:, a:a + m]).then_inc(free[b], 1)
            for p in range(KC):
                b = 4 + p % 2
                dve.wait_ge(mhi, p + 1)
                dve.scalar_tensor_tensor(wom[:, p, 1, :], bank[b][:, :], 1.0 / 16, wom[:, p, 0, :],
                                         ALU.mult, ALU.subtract).then_inc(free[b], 1)
            for p in range(KC):
                for n, ((a, m), b) in enumerate(zip(CH, SETS[p % 2])):
                    is_full(dve, "den", b, p // 2)
                    dve.tensor_tensor(qf[:, p, a:a + m], qf[:, p, a:a + m], bank[b][:, 0:m], ALU.mult)\
                        .then_inc(qn_ready, 1)
                    dve.wait_ge(qhi, 3 * p + n + 1)
                    dve.tensor_tensor(qq[:, p, 1, a:a + m], qf[:, p, a:a + m], qq[:, p, 0, a:a + m], ALU.subtract)\
                        .then_inc(free[b], 1)
            was_read(dve, "rng", 6)
            dve.wait_ge(cleared, 16)
            was_read(dve, "den", 7, 1)

            def window(a):
                s0 = dve.value_load(tab[0:1, ds(a, 1)], min_val=0, max_val=NB * ET)
                s1 = dve.value_load(tab[0:1, ds(a + 1, 1)], min_val=0, max_val=NB * ET)
                b0 = dve.value_load(tab[0:1, ds(a + 64, 1)], min_val=0, max_val=ET - TT)
                with dve.Fori(s0, s1) as n:
                    t = ((n - s0) * TT + b0).with_bounds(min_val=0, max_val=ET - TT)
                    dve.wait_ge(slots_free, n + 1)
                    keys, dests = key[:, ds(t, TT)], ring[:, ds((n % R) * (TT * N), TT * N)]
                    for v in range(TT):
                        last = dve.tensor_scalar(dests[:, v * N:v * N + N], colw[:, :, :].rearrange("p a n -> p (a n)"),
                                                 keys[:, v:v + 1], negw[:, ds(a, 1)], ALU.subtract, ALU.is_equal)
                    last.then_inc(keyed, 1)

            def window_done(a, k, u):
                for i, ((f, c), b) in enumerate(zip(WIN, SETS[u])):
                    part = (slice(None), slice(f, f + c), ds(a * B, B))
                    dve.wait_ge(chi, a * 3 + (i + 1))
                    dve.tensor_tensor(Clo[part], bank[b][0:B, 0:c * B].rearrange("p (a n) -> p a n", n=B), Chi[part],
                                      ALU.subtract).then_inc(free[b], 1)
                is_full(dve, "mix", 4 + u, k)
                dve.scalar_tensor_tensor(acc[:, ds(a, 1), :], bank[4 + u][0:B, :].rearrange("p (a n) -> p a n", a=1),
                                         2.0 ** -20, xv[:, ds(a, 1), :], ALU.mult, ALU.add).then_inc(free[4 + u], 1)

            window(0)
            with dve.Fori(0, P2 - 1) as k:
                window(k * 2 + 1)
                window_done(k * 2, k, 0)
                window(k * 2 + 2)
                window_done(k * 2 + 1, k, 1)
            window(NB - 1)
            window_done(NB - 2, P2 - 1, 0)
            window_done(NB - 1, P2 - 1, 1)
            is_full(dve, "deg", 7)
            dve.reciprocal(rc[:, :], bank[7][0:B, 0:NB]).then_inc(deg_rc, 1)
            dve.tensor_reduce(dmax[:, :], bank[7][0:B, 0:NB], AX.X, ALU.max).then_inc(free[7], 1)
            was_read(dve, "deg", 7)
            dve.tensor_scalar(large[:, :], dmax[:, :], EXACT, None, ALU.is_gt).then_inc(ind_r, 1)
            dve.wait_ge(dinv_r, 1)
            for i in range(NB):
                last = dve.tensor_scalar(diag[:, i, :], idf[0:B, 0:B], dinv[:, i:i + 1], None, ALU.mult)
            last.then_inc(diag_r, 1)
            V.mark(dve.tensor_scalar(dv64[:, :], dinv[:, :], 1.0 / S6, None, ALU.mult))
            V.link(dve.tensor_tensor(rs64[:, :], rs64[:, :], dinv[:, :], ALU.mult))
            is_full(dve, "deg", 5)
            dve.tensor_scalar(flg[0:1, 0:1], bank[5][0:1, 0:1], 0.0, None, ALU.is_gt).then_inc(free[5], 1)
            with dve.Fori(0, P2) as k:
                for u in range(2):
                    i = k * 2 + u
                    dve.wait_ge(xg_l[u], k + 1)
                    dve.tensor_scalar(xgt[:, u, :], xv[:, ds(i, 1), :].rearrange("p a n -> p (a n)"),
                                      mv[:, ds(i, 1), 0], rs64[:, ds(i, 1)],
                                      ALU.subtract, ALU.mult).then_inc(xg_t[u], 1)
                for u in range(2):
                    dve.wait_ge(xg_h[u], k + 1)
                    dve.tensor_tensor(xg[:, ds(k * 2 + u, 1), 1, :].rearrange("p a n -> p (a n)"), xgt[:, u, :],
                                      xg[:, ds(k * 2 + u, 1), 0, :].rearrange("p a n -> p (a n)"), ALU.subtract)\
                        .then_inc(xg_l[u], 1)
            for n in range(KC):
                dve.wait_ge(ghi, n + 1)
                dve.scalar_tensor_tensor(W1s[:, n, 1, :], gstage[:, n % 3, :], S6, W1s[:, n, 0, :],
                                         ALU.mult, ALU.subtract).then_inc(glo, 1)
            for b in range(3):
                was_read(dve, "dbc", b)

            def y_full(k, m):
                (a, n), b = CH[m % 3], SETS[m // 3][m % 3]
                is_full(dve, "l1", b, k)
                dve.wait_ge(y_l[m % 2], k * 3 + (m // 2 + 1))
                dve.tensor_tensor(ftmp[:, m % 2, 0:n], bank[b][:, 0:n], dbc[:, a:a + n], ALU.mult)\
                    .then_inc(free[b], 1)

            def y_low(k, m):
                (a, n), b = CH[m % 3], SETS[m // 3][m % 3]
                dve.wait_ge(y_h[m % 2], k * 3 + (m // 2 + 1))
                c = ds(k * 2 + m // 3, 1)
                dve.tensor_tensor(y1T[:, c, 1, a:a + n].rearrange("p a n -> p (a n)"), ftmp[:, m % 2, 0:n],
                                  y1T[:, c, 0, a:a + n].rearrange("p a n -> p (a n)"), ALU.subtract)\
                    .then_inc(y_l[m % 2], 1)

            with dve.Fori(0, 2) as k:
                for m in range(6):
                    y_full(k, m)
                    if m:
                        y_low(k, m - 1)
                y_low(k, 5)
            for n in range(KC, KC + HC // 2):
                dve.wait_ge(ghi, n + 1)
                c = 2 * (n - KC)
                dve.scalar_tensor_tensor(W2s[:, c:c + 2, 1, :], gstage[:, n % 3, :].rearrange("p (c n) -> p c n", c=2),
                                         S6, W2s[:, c:c + 2, 0, :], ALU.mult, ALU.subtract).then_inc(glo, 1)
            dve.wait_ge(small_in, 48)
            dve.tensor_scalar(gm64[:, :], gam[:, :], S6, None, ALU.mult).then_inc(gms, 1)
            dve.wait_ge(glo, KC + HC // 2)
            with dve.Fori(0, HC // 2) as k:
                for m in range(6):
                    a, n = CH[m % 3]
                    c = ds(k * 2 + m // 3, 1)
                    dve.wait_ge(h_h[m % 2], k * 3 + (m // 2 + 1))
                    dve.tensor_tensor(hTlo[:, c, a:a + n].rearrange("p a n -> p (a n)"), ftmp[:, m % 2, 0:n],
                                      hThi[:, c, a:a + n].rearrange("p a n -> p (a n)"), ALU.subtract)\
                        .then_inc(h_l[m % 2], 1)
            with dve.Fori(0, P2) as k:
                for u in range(2):
                    i = k * 2 + u
                    dve.wait_ge(h2hi[u], k + 1)
                    dve.scalar_tensor_tensor(h2[:, ds(i, 1), 1, :].rearrange("p a n -> p (a n)"), bank[4 + u][0:B, :],
                                             dv64[:, ds(i, 1)],
                                             h2[:, ds(i, 1), 0, :].rearrange("p a n -> p (a n)"),
                                             ALU.mult, ALU.subtract).then_inc(free[4 + u], 1)
            dve.wait_ge(bias_added, NB)

            def logit_row(i):
                u, k = i % 2, i // 2
                is_full(dve, "gate", 6 + u, k)
                dve.tensor_copy(lg[:, i, :], bank[6 + u][0:B, 0:EX]).then_inc(free[6 + u], 1)

            def norm(u, x, o):
                s = sm[:, u, :]
                V.link(dve.bn_stats(s[:, o:o + 6], x))
                V.link(dve.bn_aggr(s[:, o + 6:o + 8], s[:, o:o + 6]))
                V.link(dve.tensor_scalar(s[:, o + 8:o + 9], s[:, o + 7:o + 8], EPS, None, ALU.add))
                dve.reciprocal(s[:, o + 8:o + 9], s[:, o + 8:o + 9]).then_inc(var_r[u], 1)

            for i in range(NB):
                u, k = i % 2, i // 2
                s = sm[:, u, :]
                is_full(dve, "l2", u, k)
                dve.scalar_tensor_tensor(acc[:, i, :], bank[u][0:B, :], dv64[:, i:i + 1], acc[:, i, :],
                                         ALU.mult, ALU.add).then_inc(free[u], 1)
                was_read(dve, "l2", u, k)
                norm(u, acc[:, i, :], 0)
                dve.wait_ge(rstd_r[u], 2 * k + 1)
                dve.wait_ge(full[2 + u], told["xmT", 2 + u] + k)
                dve.tensor_scalar(xm[:, u, :], acc[:, i, :], s[:, 6:7], s[:, 9:10], ALU.subtract, ALU.mult)\
                    .then_inc(xm_r[u], 1)
                dve.wait_ge(xm_r[u], k + 1)
                norm(u, xm[:, u, :], 10)
                dve.wait_ge(rstd_r[u], 2 * k + 2)
                dve.tensor_scalar(xet[:, u, :], xm[:, u, :], s[:, 16:17], s[:, 19:20], ALU.subtract, ALU.mult)\
                    .then_inc(xe_r[u], 1)
                dve.wait_ge(xe_h[u], k + 1)
                dve.tensor_tensor(xe[:, i, 1, :], xet[:, u, :], xe[:, i, 0, :], ALU.subtract).then_inc(xe_done, 1)
                if i:
                    logit_row(i - 1)
            logit_row(NB - 1)
            was_read(dve, "gate", 6, P2 - 1)
            was_read(dve, "gate", 7, P2 - 1)

            def r(n):
                return rt[:, n, :, :]

            def col(n):
                return rt[:, n, :, 0]

            def wide(a):
                return a.rearrange("p (t e) -> p t e", e=1).to_broadcast([B, NB, EX])

            V.link(dve.tensor_reduce(rs[:, :], lg[:, :, :], AX.X, ALU.max))
            V.link(dve.tensor_tensor(r(0), lg[:, :, :], wide(rs[:, :]), ALU.subtract))
            dve.tensor_scalar(r(2), r(0), 0.0, None, ALU.is_equal).then_inc(exps_in, 1)
            dve.wait_ge(exps_in, 1)
            V.link(dve.tensor_tensor(r(2), r(2), code[:, :, :], ALU.mult))
            V.link(dve.tensor_reduce(rs64[:, :], r(2), AX.X, ALU.max))
            V.link(dve.tensor_tensor(r(3), code[:, :, :], wide(rs64[:, :]), ALU.is_equal))
            dve.tensor_copy(oh16[:, :], r(3).rearrange("p t e -> p (t e)")).then_inc(picked, 1)
            dve.wait_ge(exps_out, 1)
            V.link(dve.tensor_reduce(rs[:, :], r(1), AX.X, ALU.add))
            V.link(dve.reciprocal(rc[:, :], rs[:, :]))
            V.link(dve.tensor_tensor(r(1), r(1), wide(rc[:, :]), ALU.mult))
            V.mark(dve.tensor_reduce(rs[:, :], r(1), AX.X, ALU.max))
            V.link(dve.tensor_tensor(r(4), r(1), r(3), ALU.mult))
            V.link(dve.tensor_tensor(r(4), r(1), r(4), ALU.subtract))
            V.link(dve.tensor_reduce(rc[:, :], r(4), AX.X, ALU.max))
            V.link(dve.scalar_tensor_tensor(rc[:, :], rc[:, :], 1e-9, rs[:, :], ALU.add, ALU.add))
            V.link(dve.reciprocal(rc[:, :], rc[:, :]))
            V.mark(dve.tensor_tensor(gate[:, :], rs[:, :], rc[:, :], ALU.mult))
            is_full(dve, "route", 4)
            tot = rt[:, 5, :, :].rearrange("p t e -> p (t e)")
            V.mark(dve.tensor_copy(tot.rearrange("p (e t) -> p e t", t=NB),
                                   bank[4][0:B, 64:64 + NB * EX].rearrange("p (t e) -> p e t", e=EX)))
            notfirst = rt[:, 6, :, :].rearrange("p t e -> p (t e)")
            V.link(dve.tensor_scalar(notfirst, tnum[:, :, :].rearrange("p e t -> p (e t)"), 1.0, None, ALU.min))
            cum = rt[:, 7, :, :].rearrange("p t e -> p (t e)")
            V.link(dve.tensor_tensor_scan(cum, notfirst, tot, 0.0, ALU.mult, ALU.add))
            cume = cum.rearrange("p (e t) -> p e t", t=NB)
            til, ctl = rt[:, 8, 0, 0:EX], rt[:, 8, 1, 0:EX]
            V.link(dve.tensor_scalar(til, cume[:, :, NB - 1], 1.0 / TS, 0.5 - 0.5 / TS, ALU.mult, ALU.add))
            V.link(dve.tensor_scalar(til, til, BIG, BIG, ALU.add, ALU.subtract))
            V.link(dve.tensor_tensor_scan(ctl, onf[:, 0:EX], til, 0.0, ALU.mult, ALU.add))
            V.mark(dve.tensor_tensor(til, ctl, til, ALU.subtract))
            V.link(dve.tensor_tensor(cum, cum, tot, ALU.subtract))
            V.link(dve.scalar_tensor_tensor(
                rt[:, 9, :, :].rearrange("p t e -> p (t e)").rearrange("p (e t) -> p e t", t=NB),
                til.rearrange("p (e t) -> p e t", t=1).to_broadcast([B, EX, NB]), float(TS), cume,
                ALU.mult, ALU.add))
            V.link(dve.tensor_tensor(
                r(10), rt[:, 9, :, :].rearrange("p t e -> p (t e)").rearrange("p (e t) -> p t e", t=NB),
                bank[4][0:B, 0:NB * EX].rearrange("p (t e) -> p t e", e=EX), ALU.add))
            V.link(dve.tensor_tensor(r(10), r(10), r(3), ALU.mult))
            V.link(dve.tensor_reduce(rs64[:, :], r(10), AX.X, ALU.add))
            dve.tensor_copy(slot[:, :], rs64[:, :]).then_inc(slot_r, 1)
            past = rt[0:1, 11:13, :, :].rearrange("p a t e -> p (a t e)")[:, 0:NT * (EX - 1)]\
                .rearrange("p (k e) -> p k e", e=EX - 1)
            V.link(dve.tensor_tensor(
                past, iow[0:1, 0:NT].rearrange("p (k e) -> p k e", e=1).to_broadcast([1, NT, EX - 1]),
                ctl[0:1, 0:EX - 1].rearrange("p (k e) -> p k e", k=1).to_broadcast([1, NT, EX - 1]), ALU.is_ge))
            V.link(dve.tensor_reduce(rt[0:1, 13, :, :].rearrange("p t e -> p (t e)")[:, 0:NT], past, AX.X, ALU.add))
            dve.tensor_copy(eid[0:1, :], rt[0:1, 13, :, :].rearrange("p t e -> p (t e)")[:, 0:NT])\
                .then_inc(eid_r, 1)
            with dve.Fori(0, NT // 2) as k:
                for u in range(2):
                    dve.wait_ge(hid_h[u], k + 1)
                    dve.wait_ge(full[6 + u], k + told["yo", 6 + u])
                    dve.scalar_tensor_tensor(hids[:, u, 1, :], hid[:, u, :], S6, hids[:, u, 0, :],
                                             ALU.mult, ALU.subtract).then_inc(hid_l[u], 1)
            for i in range(NB):
                dve.wait_ge(gathered[i], 16)
                dve.scalar_tensor_tensor(acc[:, i, :], gat[:, i, :], gate[:, i:i + 1], acc[:, i, :],
                                         ALU.mult, ALU.add).then_inc(fin, 1)


def kernel(x, src, dst, L0_gnn_W1, L0_gnn_b1, L0_gnn_W2, L0_gnn_b2, L0_mix_w_qkv, L0_mix_w_out, L0_mix_b_out,
           L0_ffn_w_gating, L0_ffn_gamma, L0_ffn_w1, L0_ffn_w2):
    import numpy as np
    import concourse.bacc as bacc
    from concourse import mybir
    from concourse.bass_utils import run_bass_kernel_spmd

    tiles = len(src) // 125
    arrays = {
        "x": x,
        "src": np.asarray(src).reshape(tiles, 125).T, "dst": np.asarray(dst).reshape(tiles, 125).T,
        "dst_tiles": np.asarray(dst).reshape(tiles, 125),
        "W1": L0_gnn_W1, "b1": np.asarray(L0_gnn_b1).reshape(-1, 128).T, "W2": L0_gnn_W2, "b2": L0_gnn_b2,
        "w_qkv_T": np.asarray(L0_mix_w_qkv).T, "w_out_T": np.asarray(L0_mix_w_out).T, "b_out": L0_mix_b_out,
        "w_gating": L0_ffn_w_gating, "gamma": np.asarray(L0_ffn_gamma).reshape(-1, 128).T,
        "w1": L0_ffn_w1, "w2": L0_ffn_w2,
    }
    nc = bacc.Bacc("TRN2", target_bir_lowering=False, num_devices=1)
    args = []
    for name in arrays:
        a = arrays[name] = np.ascontiguousarray(arrays[name])
        args.append(nc.dram_tensor(name, a.shape, mybir.dt.from_np(a.dtype), kind="ExternalInput").ap())
    out = nc.dram_tensor("out", (1250, 512), mybir.dt.float32, kind="ExternalOutput").ap()
    slots = nc.dram_tensor("slots", (2048, 1024), mybir.dt.float16, kind="Internal").ap()
    yslots = nc.dram_tensor("yslots", (2048, 512), mybir.dt.float32, kind="Internal").ap()
    gps_layer_kernel(nc, *args, out, slots, yslots)
    r = run_bass_kernel_spmd(nc, [arrays], core_ids=[0])
    return r.results[0]["out"]
```
